# Optimizing a Trainium2 kernel written in Bass

```python
import numpy as np
import jax
import jax.numpy as jnp

def _softmax(x, axis=-1):
    return jax.nn.softmax(x, axis=axis)

def _gelu(x):
    return jax.nn.gelu(x, approximate=True)

def _silu(x):
    return jax.nn.silu(x)

def _sigmoid(x):
    return jax.nn.sigmoid(x)

def _layernorm(x, axis=-1, eps=1e-05):
    m = jnp.mean(x, axis=axis, keepdims=True)
    v = jnp.var(x, axis=axis, keepdims=True)
    return (x - m) / jnp.sqrt(v + eps)

def _scatter_add(tgt, idx, src, axis=0):
    return tgt.at[idx].add(src)

def _segment_sum(src, seg, n):
    return jax.ops.segment_sum(src, seg, n)
kernel_name = 'mk_cond_resid_d1_seqx_r8_a8d91d'

def setup_inputs(seed: int=0):
    np.random.seed(seed)
    _w = jnp.asarray

    def _rec_inputs():
        import jax
        import jax.numpy as jnp
        _rk = jax.random.key(seed)
        x = -0.000125 + 0.9999 * jax.random.normal(jax.random.fold_in(_rk, 1), (128, 32, 512), jnp.float32)
        _lenS = 32 - jax.random.randint(jax.random.fold_in(_rk, 7), (128,), 0, max(1, 32 // 4) + 1, jnp.int32)
        _lenS2 = 32 - jax.random.randint(jax.random.fold_in(_rk, 8), (128,), 0, max(1, 32 // 4) + 1, jnp.int32)
        itok_B_3_7 = jax.random.randint(jax.random.fold_in(_rk, 11), (128,), 3, 8, jnp.int32)
        return (x, itok_B_3_7)
    x, itok_B_3_7 = _rec_inputs()

    def _L0_cond_setup():
        import jax, jax.numpy as jnp
        import numpy as np
        MAX_LORAS, OUT, IN = (8, 512, 512)
        B, S = (4, 256)
        key = jax.random.key(seed)
        k1, k2, k3 = jax.random.split(key, 3)
        x = jax.random.normal(k1, (B, S, IN), dtype=jnp.float32)
        weight = jax.random.normal(k2, (MAX_LORAS, OUT, IN), dtype=jnp.float32) * 0.02
        adapter_ids = jax.random.randint(k3, (B,), 0, MAX_LORAS, dtype=jnp.int32)
        return {'x': x, 'weight': weight, 'adapter_ids': adapter_ids}
    _L0_cond_all = _L0_cond_setup()
    _L0_cond_in = {k: v for k, v in _L0_cond_all.items() if k in ('weight',)}
    del _L0_cond_all
    return {'x': x, 'itok_B_3_7': itok_B_3_7, 'L0_cond_weight': _L0_cond_in['weight']}

def reference(x, itok_B_3_7, L0_cond_weight):
    import jax
    import jax.numpy as jnp

    def _L0_cond_ref(x, weight, adapter_ids):
        import jax, jax.numpy as jnp
        import numpy as np
        MAX_LORAS, OUT, IN = (8, 512, 512)
        B, S = (4, 256)
        w = weight[adapter_ids]
        return jnp.einsum('bsi,boi->bso', x, w)
    x = x + _L0_cond_ref(x, L0_cond_weight, itok_B_3_7)
    return x

_drawn_inputs = setup_inputs


def setup_inputs(seed=0):
    import zlib

    import numpy as np

    out = dict(_drawn_inputs(seed))
    spreads = {}
    factors = {}
    for name, (base, spread) in spreads.items():
        noise = np.random.default_rng([zlib.crc32(name.encode()), seed]).standard_normal(out[name].shape)
        drawn = base * np.exp(spread * noise) if base else spread * noise
        out[name] = jnp.asarray(drawn.astype(out[name].dtype))
    for name, factor in factors.items():
        out[name] = (out[name] * factor).astype(out[name].dtype)
    return out
```

```python
from contextlib import ExitStack

import numpy as np

import concourse.bass as bass
from concourse import mybir
from concourse.alu_op_type import AluOpType as ALU

B, S, D, ADAPTERS = 128, 32, 512, 8
P = 128
SEQS = P // S
MAX_TILES = (B + ADAPTERS * (SEQS - 1)) // SEQS
MIN_TILES = B // SEQS
UNROLL = 4
ROUNDS = MIN_TILES // UNROLL
TABLE = MAX_TILES + UNROLL + 2
CHUNKS = D // P
Q = 32
KG = P // Q
HALVES = 2
HO = D // HALVES
SUBS = 2
BANK = 512
CREDIT = 8
NO_ROW = B * S


def routed_adapter_kernel(nc, x, ids, weight, out):
    f32, f32r, bf16, i32 = (mybir.dt.float32, mybir.dt.float32r, mybir.dt.bfloat16, mybir.dt.int32)
    COPY = mybir.ActivationFunctionType.Copy
    x_rows = x.rearrange("b s d -> (b s) d")
    out_rows = out.rearrange("b s d -> (b s) d")
    weight_v = weight.rearrange("a (h m o) (k i) -> a h k o m i", h=HALVES, o=Q, k=KG)

    ctx = ExitStack()
    with ctx:
        def sb(name, shape, dt):
            return ctx.enter_context(nc.sbuf_tensor(name, shape, dt))

        def ps(name, shape, dt):
            return ctx.enter_context(nc.psum_tensor(name, shape, dt))

        def sem(name):
            return ctx.enter_context(nc.semaphore(name))

        w_hi = sb("w_hi", [P, ADAPTERS, CHUNKS, D], f32r)
        w_lo = sb("w_lo", [P, ADAPTERS, CHUNKS, D], f32r)
        w_raw = [sb(f"w_raw{h}", [P, HO // Q, P], f32) for h in range(HALVES)]
        x_tile = [sb(f"x_tile{s}", [P, D], f32) for s in range(UNROLL)]
        out_tile = [sb(f"out_tile{s}", [P, D], f32) for s in range(UNROLL)]
        xt_hi = [sb(f"xt_hi{s}", [P, CHUNKS, P], f32r) for s in range(2)]
        xt_lo = [sb(f"xt_lo{s}", [P, CHUNKS, P], f32r) for s in range(2)]
        row_of = sb("row_of", [P, TABLE], i32)
        row_now = [sb(f"row_now{s}", [P, 2], i32) for s in range(UNROLL)]
        tables = sb("tables", [1, 3, TABLE], i32)
        tile_count = sb("tile_count", [1, 1], i32)
        identity = sb("identity", [P, P], f32)
        earlier = sb("earlier", [P, P], bf16)
        ones = sb("ones", [P, P], bf16)
        adapter_no = sb("adapter_no", [P, ADAPTERS], f32)
        tile_no = sb("tile_no", [P, TABLE], f32)
        place_no = sb("place_no", [P, P], f32)
        seq_off = sb("seq_off", [P, 1], f32)
        row_in_seq = sb("row_in_seq", [P, 1], i32)
        row_base = sb("row_base", [P, 1], f32)
        ids_i = sb("ids_i", [P, 1], i32)
        idf = sb("idf", [P, 1], f32)
        is_own = sb("is_own", [P, ADAPTERS], bf16)
        is_lower = sb("is_lower", [P, ADAPTERS], f32)
        tiles_i = sb("tiles_i", [P, ADAPTERS], i32)
        prod = sb("prod", [P, ADAPTERS], f32)
        start_tile = sb("start_tile", [P, 1], f32)
        rank = sb("rank", [P, 1], f32)
        full_i = sb("full_i", [P, 1], i32)
        full = sb("full", [P, 1], f32)
        own_tile = sb("own_tile", [P, 1], f32)
        place = sb("place", [P, 1], f32)
        opens = sb("opens", [P, 2], bf16)
        in_tile = sb("in_tile", [P, TABLE], bf16)
        by_tile = sb("by_tile", [P, TABLE], bf16)
        seq_at = sb("seq_at", [P, P], bf16)

        xt_ps = [ps(f"xt_ps{s}", [P, CHUNKS, P], f32) for s in range(2)]
        out_ps = [ps(f"out_ps{s}", [P, D], f32) for s in range(2)]
        w_ps = [ps(f"w_ps{s}", [P, SUBS, HO], f32) for s in range(2)]
        route_ps = ps("route_ps", [P, BANK], f32)
        table_ps = ps("table_ps", [P, BANK], f32)

        ids_loaded = sem("ids_loaded")
        constants_ready = sem("constants_ready")
        triangle_ready = sem("triangle_ready")
        buffers_clean = sem("buffers_clean")
        own_ready = sem("own_ready")
        ranks_ready = sem("ranks_ready")
        factors_ready = sem("factors_ready")
        tables_summed = sem("tables_summed")
        rows_ready = sem("rows_ready")
        tables_ready = sem("tables_ready")
        route_step = sem("route_step")
        row_copied = sem("row_copied")
        x_loaded = [sem(f"x_loaded{s}") for s in range(UNROLL)]
        stored = [sem(f"stored{s}") for s in range(UNROLL)]
        w_loaded = [sem(f"w_loaded{h}") for h in range(HALVES)]
        xt_ready = sem("xt_ready")
        hi_ready = sem("hi_ready")
        lo_ready = sem("lo_ready")
        product_ready = sem("product_ready")
        out_added = sem("out_added")
        w_turned = sem("w_turned")
        w_hi_ready = sem("w_hi_ready")
        w_lo_ready = sem("w_lo_ready")

        def done(n):
            return n + CREDIT

        SUB_PER_W = HALVES * SUBS

        block = ctx.enter_context(nc.Block())

        @block.sync
        def _(sp):
            for s in (xt_ready, hi_ready, lo_ready, product_ready, out_added,
                      w_turned, w_hi_ready, w_lo_ready):
                sp.sem_inc(s, CREDIT)
            sp.dma_start(ids_i[:, :], ids.rearrange("(b o) -> b o", o=1)).then_inc(ids_loaded, 16)
            sp.wait_ge(tables_ready, 1)
            with sp.Fori(0, MAX_TILES) as t:
                opens_adapter = sp.value_load(tables[0:1, 2, bass.ds(t, 1)], min_val=0, max_val=1)
                with sp.If(opens_adapter > 0):
                    a = sp.value_load(tables[0:1, 0, bass.ds(t, 1)], min_val=0, max_val=ADAPTERS - 1)
                    nth = sp.value_load(tables[0:1, 1, bass.ds(t, 1)], min_val=1, max_val=ADAPTERS)
                    for h in range(HALVES):
                        sp.wait_ge(w_turned, done(nth * SUB_PER_W - 2 * SUB_PER_W + SUBS * (h + 1)))
                        for k in range(KG):
                            sp.dma_start(w_raw[h][Q * k:Q * k + Q, :, :],
                                         weight_v[bass.ds(a, 1), h, k, :, :, :].rearrange("a o m i -> (a o) m i")
                                         ).then_inc(w_loaded[h], 16)

        @block.gpsimd
        def _(pool):
            nc.gpsimd.memset(ones[:, :], 1.0).then_inc(constants_ready, 1)
            nc.gpsimd.memset(identity[:, :], 0.0).then_inc(constants_ready, 1)
            nc.gpsimd.iota(adapter_no[:, :], [[1, ADAPTERS]], base=0, channel_multiplier=0,
                           allow_small_or_imprecise_dtypes=True).then_inc(constants_ready, 1)
            pool.wait_ge(constants_ready, 3)
            nc.gpsimd.affine_select(out=earlier[:, :], in_=ones[:, :], compare_op=ALU.is_ge, fill=0.0,
                                    base=-1, pattern=[[1, P]], channel_multiplier=-1).then_inc(triangle_ready, 1)
            nc.gpsimd.iota(tile_no[:, :], [[1, TABLE]], base=0, channel_multiplier=0,
                           allow_small_or_imprecise_dtypes=True).then_inc(constants_ready, 1)
            nc.gpsimd.iota(place_no[:, :], [[1, SEQS], [0, S]], base=0, channel_multiplier=0,
                           allow_small_or_imprecise_dtypes=True).then_inc(constants_ready, 1)
            nc.gpsimd.iota(seq_off[:, :], [[0, 1]], base=-B, channel_multiplier=1,
                           allow_small_or_imprecise_dtypes=True).then_inc(constants_ready, 1)
            nc.gpsimd.iota(row_in_seq[:, :], [[0, 1]], base=0, channel_multiplier=1).then_inc(constants_ready, 1)
            nc.gpsimd.affine_select(out=identity[:, :], in_=identity[:, :], compare_op=ALU.not_equal, fill=1.0,
                                    base=0, pattern=[[-1, P]], channel_multiplier=1).then_inc(constants_ready, 1)

            def gather(s, rows):
                nc.gpsimd.indirect_dma_start(
                    out=x_tile[s][:, :], out_offset=None, in_=x_rows,
                    in_offset=bass.IndirectOffsetOnAxis(ap=rows, axis=0),
                    bounds_check=NO_ROW - 1, oob_is_err=False).then_inc(x_loaded[s], 16)

            def scatter(s, rows):
                nc.gpsimd.indirect_dma_start(
                    out=out_rows, out_offset=bass.IndirectOffsetOnAxis(ap=rows, axis=0),
                    in_=out_tile[s][:, :], in_offset=None,
                    bounds_check=NO_ROW - 1, oob_is_err=False).then_inc(stored[s], 16)

            def take_rows(t, s, round_no):
                pool.wait_ge(stored[s], 16 * round_no)
                nc.gpsimd.tensor_copy(row_now[s][:, :], row_of[:, bass.ds(t, 2, UNROLL)]).then_inc(row_copied, 1)

            pool.wait_ge(rows_ready, 1)
            pool.wait_ge(buffers_clean, UNROLL)
            for s in range(UNROLL):
                gather(s, row_of[:, s:s + 1])
            take_rows(0, 0, 0)

            def step(t, s, round_no):
                pool.wait_ge(out_added, done(t + 1))
                pool.wait_ge(row_copied, t + 1)
                if not (isinstance(t, int) and t + 1 == MAX_TILES):
                    take_rows(t + 1, (s + 1) % UNROLL, round_no + (s + 1) // UNROLL)
                scatter(s, row_now[s][:, 0:1])
                if not (isinstance(t, int) and t + UNROLL >= MAX_TILES):
                    gather(s, row_now[s][:, 1:2])

            with pool.Fori(0, ROUNDS) as r:
                for s in range(UNROLL):
                    step(r * UNROLL + s, s, r)
            tiles = pool.value_load(tile_count[0:1, 0:1], min_val=MIN_TILES, max_val=MAX_TILES)
            for t in range(MIN_TILES, MAX_TILES):
                with pool.If(tiles > t):
                    step(t, t % UNROLL, t // UNROLL)
                    if t + UNROLL < MAX_TILES:
                        pool.wait_ge(x_loaded[t % UNROLL], 16 * (t // UNROLL + 2))
            for s in range(UNROLL):
                pool.wait_ge(stored[s], 16 * ((tiles + (UNROLL - 1 - s)) >> 2))
                pool.wait_ge(x_loaded[s], 16 * (ROUNDS + 1))

        @block.scalar
        def _(act):
            def split_x(t, s):
                act.wait_ge(xt_ready, done(t + 1))
                act.wait_ge(product_ready, done(t - 1))
                nc.scalar.activation(xt_hi[s % 2][:, :, :], xt_ps[s % 2][:, :, :], COPY).then_inc(hi_ready, 1)

            def weight_half(h, a, nth):
                for u in range(SUBS):
                    sub = SUBS * h + u
                    act.wait_ge(w_turned, done(nth * SUB_PER_W - SUB_PER_W + sub + 1))
                    nc.scalar.activation(w_hi[:, bass.ds(a, 1), SUBS * u:SUBS * u + SUBS, h * HO:(h + 1) * HO].rearrange("p a c o -> p (a c) o"),
                                         w_ps[sub % 2][:, :, :], COPY).then_inc(w_hi_ready, 1)

            def weight(t, halves):
                opens_adapter = act.value_load(tables[0:1, 2, bass.ds(t, 1)], min_val=0, max_val=1)
                with act.If(opens_adapter > 0):
                    a = act.value_load(tables[0:1, 0, bass.ds(t, 1)], min_val=0, max_val=ADAPTERS - 1)
                    nth = act.value_load(tables[0:1, 1, bass.ds(t, 1)], min_val=1, max_val=ADAPTERS)
                    for h in halves:
                        weight_half(h, a, nth)

            act.wait_ge(tables_ready, 1)
            weight(0, (0, 1))
            weight(1, (0, 1))
            weight(2, (0,))
            split_x(0, 0)

            def step(t, s, last):
                if not last:
                    split_x(t + 1, s + 1)
                weight(t + 2, (1,))
                weight(t + 3, (0,))

            with act.Fori(0, MIN_TILES, UNROLL) as t0:
                for s in range(UNROLL):
                    step(t0 + s, s, False)
            tiles = act.value_load(tile_count[0:1, 0:1], min_val=MIN_TILES, max_val=MAX_TILES)
            for t in range(MIN_TILES, MAX_TILES):
                with act.If(tiles > t):
                    step(t, t % UNROLL, t + 1 == MAX_TILES)

        @block.vector
        def _(dve):
            steps = [0]

            def link(ins):
                steps[0] += 1
                ins.then_inc(route_step, 1)
                dve.wait_ge(route_step, steps[0])

            for s in range(UNROLL):
                nc.vector.memset(x_tile[s][:, :], 0.0).then_inc(buffers_clean, 1)
            dve.wait_ge(ids_loaded, 16)
            link(nc.vector.tensor_copy(idf[:, :], ids_i[:, :]))
            dve.wait_ge(constants_ready, 3)
            link(nc.vector.tensor_scalar(is_own[:, :], adapter_no[:, :], idf[:, 0:1], None, ALU.is_equal))
            nc.vector.tensor_scalar(is_lower[:, :], adapter_no[:, :], idf[:, 0:1], None,
                                    ALU.is_lt).then_inc(own_ready, 1)
            dve.wait_ge(constants_ready, 8)
            link(nc.vector.tensor_scalar(row_in_seq[:, :], row_in_seq[:, :], S - 1, None, ALU.bitwise_and))
            link(nc.vector.tensor_scalar(row_base[:, :], row_in_seq[:, :], float(NO_ROW), None, ALU.add))
            ranks = route_ps[:, 0:ADAPTERS]
            counts = route_ps[:, ADAPTERS:2 * ADAPTERS]
            dve.wait_ge(ranks_ready, 1)
            link(nc.vector.tensor_scalar(tiles_i[:, :], counts, float(SEQS - 1), None, ALU.add))
            link(nc.vector.tensor_scalar(tiles_i[:, :], tiles_i[:, :], 2, None, ALU.arith_shift_right))
            link(nc.vector.tensor_tensor_reduce(out=prod[:, :], in0=is_lower[:, :], in1=tiles_i[:, :], scale=1.0,
                                                scalar=0.0, op0=ALU.mult, op1=ALU.add, accum_out=start_tile[:, 0:1]))
            link(nc.vector.tensor_tensor_reduce(out=prod[:, :], in0=ranks, in1=is_own[:, :], scale=1.0,
                                                scalar=0.0, op0=ALU.mult, op1=ALU.add, accum_out=rank[:, 0:1]))
            link(nc.vector.tensor_copy(full_i[:, :], rank[:, :]))
            link(nc.vector.tensor_scalar(full_i[:, :], full_i[:, :], 2, None, ALU.arith_shift_right))
            link(nc.vector.tensor_copy(full[:, :], full_i[:, :]))
            link(nc.vector.tensor_tensor(own_tile[:, :], start_tile[:, :], full[:, :], ALU.add))
            link(nc.vector.scalar_tensor_tensor(out=place[:, :], in0=full[:, :], scalar=-float(SEQS), in1=rank[:, :],
                                                op0=ALU.mult, op1=ALU.add))
            nc.vector.tensor_scalar(in_tile[:, :], tile_no[:, :], own_tile[:, 0:1], None, ALU.is_equal)
            nc.vector.tensor_scalar(seq_at[:, :], place_no[:, :], place[:, 0:1], seq_off[:, 0:1], ALU.is_equal, ALU.mult)
            nc.vector.tensor_scalar(by_tile[:, :], tile_no[:, :], own_tile[:, 0:1], None, ALU.is_ge)
            nc.vector.tensor_scalar(opens[:, 0:1], place[:, :], 0.0, idf[:, 0:1], ALU.is_equal, ALU.mult)
            nc.vector.tensor_scalar(opens[:, 1:2], rank[:, :], 0.0, None, ALU.is_equal).then_inc(factors_ready, 1)
            dve.wait_ge(tables_summed, 1)
            nc.vector.tensor_scalar(row_of[:, :], route_ps[:, 64:64 + TABLE], float(S), row_base[:, 0:1],
                                    ALU.mult, ALU.add).then_inc(rows_ready, 1)
            nc.vector.tensor_copy(tables[0:1, :, :], table_ps[0:1, 0:3 * TABLE].rearrange("p (n t) -> p n t", n=3))
            link(nc.vector.tensor_reduce(out=full[0:1, :], in_=tiles_i[0:1, :], axis=mybir.AxisListType.X, op=ALU.add))
            nc.vector.tensor_copy(tile_count[0:1, :], full[0:1, :]).then_inc(tables_ready, 1)

            def split_x(t, s):
                dve.wait_ge(hi_ready, done(t + 1))
                nc.vector.tensor_tensor(xt_lo[s % 2][:, :, :], xt_ps[s % 2][:, :, :],
                                        xt_hi[s % 2][:, :, :].bitcast(f32), ALU.subtract).then_inc(lo_ready, 1)

            def weight_half(h, a, nth):
                base = nth * SUB_PER_W - SUB_PER_W
                dve.wait_ge(w_loaded[h], nth * (16 * KG))
                for u in range(SUBS):
                    sub = SUBS * h + u
                    dve.wait_ge(w_lo_ready, done(base + sub - 1))
                    nc.vector.transpose(
                        w_ps[sub % 2][:, :, :].rearrange("p c (m o) -> p c m o", o=Q),
                        w_raw[h][:, :, :].rearrange("p m (q c) -> p c m q", c=CHUNKS)[:, SUBS * u:SUBS * (u + 1), :, :]
                    ).then_inc(w_turned, 1)
                for u in range(SUBS):
                    sub = SUBS * h + u
                    dve.wait_ge(w_hi_ready, done(base + sub + 1))
                    chunk = (slice(None), bass.ds(a, 1), slice(SUBS * u, SUBS * u + SUBS), slice(h * HO, (h + 1) * HO))
                    nc.vector.tensor_tensor(w_lo[chunk].rearrange("p a c o -> p (a c) o"), w_ps[sub % 2][:, :, :],
                                            w_hi[chunk].rearrange("p a c o -> p (a c) o").bitcast(f32),
                                            ALU.subtract).then_inc(w_lo_ready, 1)

            def weight(t, halves):
                opens_adapter = dve.value_load(tables[0:1, 2, bass.ds(t, 1)], min_val=0, max_val=1)
                with dve.If(opens_adapter > 0):
                    a = dve.value_load(tables[0:1, 0, bass.ds(t, 1)], min_val=0, max_val=ADAPTERS - 1)
                    nth = dve.value_load(tables[0:1, 1, bass.ds(t, 1)], min_val=1, max_val=ADAPTERS)
                    for h in halves:
                        weight_half(h, a, nth)

            dve.wait_ge(tables_ready, 1)
            weight(0, (0, 1))
            weight(1, (0, 1))
            weight(2, (0,))
            split_x(0, 0)

            def step(t, s, round_no, last):
                if not last:
                    split_x(t + 1, s + 1)
                weight(t + 2, (1,))
                weight(t + 3, (0,))
                dve.wait_ge(product_ready, done(t + 1))
                dve.wait_ge(stored[s], round_no * 16)
                nc.vector.tensor_tensor(out_tile[s][:, :], out_ps[s % 2][:, :], x_tile[s][:, :],
                                        ALU.add).then_inc(out_added, 1)

            with dve.Fori(0, ROUNDS) as r:
                for s in range(UNROLL):
                    step(r * UNROLL + s, s, r, False)
            tiles = dve.value_load(tile_count[0:1, 0:1], min_val=MIN_TILES, max_val=MAX_TILES)
            for t in range(MIN_TILES, MAX_TILES):
                with dve.If(tiles > t):
                    step(t, t % UNROLL, t // UNROLL, t + 1 == MAX_TILES)

        @block.tensor
        def _(pe):
            pe.wait_ge(constants_ready, 1)
            pe.wait_ge(triangle_ready, 1)
            pe.wait_ge(own_ready, 1)
            nc.tensor.matmul(route_ps[:, 0:ADAPTERS], earlier[:, :], is_own[:, :], start=True, stop=True)
            nc.tensor.matmul(route_ps[:, ADAPTERS:2 * ADAPTERS], ones[:, :], is_own[:, :],
                             start=True, stop=True).then_inc(ranks_ready, 1)
            pe.wait_ge(factors_ready, 1)
            nc.tensor.matmul(route_ps[:, 64:64 + TABLE], seq_at[:, :], in_tile[:, :], start=True, stop=True)
            for n, (factor, by) in enumerate(((0, in_tile), (1, by_tile), (1, in_tile))):
                last = nc.tensor.matmul(table_ps[0:1, n * TABLE:(n + 1) * TABLE], opens[:, factor:factor + 1], by[:, :],
                                        start=True, stop=True)
            last.then_inc(tables_summed, 1)

            def transpose_x(t, s, round_no):
                pe.wait_ge(x_loaded[s], round_no * 16 + 16)
                pe.wait_ge(lo_ready, done(t - 1))
                rows = x_tile[s][:, :].rearrange("r (j c) -> r c j", c=CHUNKS)
                for c in range(CHUNKS):
                    last = nc.tensor.transpose(xt_ps[s % 2][:, c, :], rows[:, c, :], identity[:, :])
                last.then_inc(xt_ready, 1)

            def multiply(t, s):
                a = pe.value_load(tables[0:1, 0, bass.ds(t, 1)], min_val=0, max_val=ADAPTERS - 1)
                nth = pe.value_load(tables[0:1, 1, bass.ds(t, 1)], min_val=1, max_val=ADAPTERS)
                pe.wait_ge(w_lo_ready, done(nth * SUB_PER_W))
                pe.wait_ge(lo_ready, done(t + 1))
                pe.wait_ge(out_added, done(t - 1))
                for c in range(CHUNKS):
                    for n, (left, right) in enumerate(((xt_hi, w_hi), (xt_hi, w_lo), (xt_lo, w_hi))):
                        last = nc.tensor.matmul(out_ps[s % 2][:, :], left[s % 2][:, c, :],
                                                right[:, bass.ds(a, 1), c, :].rearrange("p a o -> p (a o)"),
                                                start=(c == 0 and n == 0), stop=(c == CHUNKS - 1 and n == 2))
                last.then_inc(product_ready, 1)

            pe.wait_ge(constants_ready, 8)
            pe.wait_ge(tables_ready, 1)
            transpose_x(0, 0, 0)

            def step(t, s, round_no, last):
                if not last:
                    transpose_x(t + 1, (s + 1) % UNROLL, round_no + (s + 1) // UNROLL)
                multiply(t, s)

            with pe.Fori(0, ROUNDS) as r:
                for s in range(UNROLL):
                    step(r * UNROLL + s, s, r, False)
            tiles = pe.value_load(tile_count[0:1, 0:1], min_val=MIN_TILES, max_val=MAX_TILES)
            for t in range(MIN_TILES, MAX_TILES):
                with pe.If(tiles > t):
                    step(t, t % UNROLL, t // UNROLL, t + 1 == MAX_TILES)


def kernel(**inputs):
    import concourse.bacc as bacc
    from concourse.bass_utils import run_bass_kernel_spmd

    nc = bacc.Bacc("TRN2", target_bir_lowering=False, num_devices=1)
    arrays, args = {}, []
    for name in ("x", "itok_B_3_7", "L0_cond_weight"):
        a = np.ascontiguousarray(inputs[name])
        arrays[f"in_{name}"] = a
        args.append(nc.dram_tensor(f"in_{name}", a.shape, mybir.dt.from_np(a.dtype), kind="ExternalInput").ap())
    out = nc.dram_tensor("out", (B, S, D), mybir.dt.float32, kind="ExternalOutput").ap()
    routed_adapter_kernel(nc, *args, out)
    result = run_bass_kernel_spmd(nc, [arrays], core_ids=[0])
    return result.results[0]["out"]
```

```python
from contextlib import ExitStack

import numpy as np

import concourse.bass as bass
from concourse import mybir
from concourse.alu_op_type import AluOpType as ALU

B, S, D, ADAPTERS = 128, 32, 512, 8
P = 128
SEQS = P // S
MIN_TILES = B // SEQS
MAX_TILES = (B + ADAPTERS * (SEQS - 1)) // SEQS
UNROLL = 4
AHEAD = UNROLL
TABLE = MAX_TILES + AHEAD
CHUNKS = D // P
Q = 32
KG = P // Q
HALVES = 2
HO = D // HALVES
QUARTERS = 4
W_ROUNDS = ADAPTERS - 1
CREDIT = 4
NO_ROW = B * S
KEY = ADAPTERS


def routed_adapter_kernel(nc, x, ids, weight, out):
    f32, f32r, bf16, i32 = (mybir.dt.float32, mybir.dt.float32r, mybir.dt.bfloat16, mybir.dt.int32)
    COPY = mybir.ActivationFunctionType.Copy
    x_rows = x.rearrange("b s d -> (b s) d")
    out_rows = out.rearrange("b s d -> (b s) d")
    weight_v = weight.rearrange("a (h m o) (k i) -> a h k o m i", h=HALVES, o=Q, k=KG)

    ctx = ExitStack()
    with ctx:
        def sb(name, shape, dt):
            return ctx.enter_context(nc.sbuf_tensor(name, shape, dt))

        def ps(name, shape, dt):
            return ctx.enter_context(nc.psum_tensor(name, shape, dt))

        def sem(name):
            return ctx.enter_context(nc.semaphore(name))

        w_hi = sb("w_hi", [P, ADAPTERS, CHUNKS, D], f32r)
        w_lo = sb("w_lo", [P, ADAPTERS, CHUNKS, D], f32r)
        w_raw = [sb(f"w_raw{h}", [P, HO // Q, P], f32) for h in range(HALVES)]
        x_tile = [sb(f"x_tile{s}", [P, D], f32) for s in range(UNROLL)]
        out_tile = [sb(f"out_tile{s}", [P, D], f32) for s in range(UNROLL)]
        xt_hi = [sb(f"xt_hi{s}", [P, CHUNKS, P], f32r) for s in range(2)]
        xt_lo = [sb(f"xt_lo{s}", [P, CHUNKS, P], f32r) for s in range(2)]
        row_of = sb("row_of", [P, TABLE], i32)
        row_now = [sb(f"row_now{s}", [P, 2], i32) for s in range(UNROLL)]
        rank_of_tile = sb("rank_of_tile", [1, TABLE], i32)
        adapter_of_rank = sb("adapter_of_rank", [1, ADAPTERS], i32)
        tile_count = sb("tile_count", [1, 1], i32)
        identity = sb("identity", [P, P], f32)
        earlier = sb("earlier", [P, P], bf16)
        ones = sb("ones", [P, P], bf16)
        adapter_no = sb("adapter_no", [P, ADAPTERS], f32)
        slot_no = sb("slot_no", [P, SEQS * TABLE], f32)
        seq_off = sb("seq_off", [P, P], bf16)
        row_in_seq = sb("row_in_seq", [P, 1], i32)
        row_base = sb("row_base", [P, 1], f32)
        ids_i = sb("ids_i", [P, 1], i32)
        is_own = sb("is_own", [P, ADAPTERS], bf16)
        tiles_i = sb("tiles_i", [P, ADAPTERS], i32)
        key = sb("key", [P, ADAPTERS], f32)
        sorted_key = sb("sorted_key", [1, ADAPTERS], i32)
        masked = sb("masked", [P, ADAPTERS], f32)
        own_key = sb("own_key", [P, 1], f32)
        own_rank = sb("own_rank", [P, 1], f32)
        own_rank_b = sb("own_rank_b", [P, 1], bf16)
        start_slot = sb("start_slot", [P, 1], f32)
        slot = sb("slot", [P, 1], f32)
        in_slot = sb("in_slot", [P, SEQS * TABLE], bf16)
        tiles_f = sb("tiles_f", [1, 1], f32)
        warm = sb("warm", [1, 1], f32)

        xt_ps = [ps(f"xt_ps{s}", [P, CHUNKS, P], f32) for s in range(2)]
        w_ps = [ps(f"w_ps{s}", [P, 2, HO], f32) for s in range(2)]
        out_ps = [ps(f"out_ps{s}", [P, D], f32) for s in range(UNROLL)]
        route_ps = out_ps[UNROLL - 1]
        earlier_own = route_ps[:, 0:ADAPTERS]
        counts = route_ps[:, ADAPTERS:2 * ADAPTERS]
        seq_of_slot = route_ps[:, 2 * ADAPTERS:2 * ADAPTERS + SEQS * TABLE]
        rank_sums = out_ps[UNROLL - 2][0:1, 0:TABLE]

        ids_loaded = sem("ids_loaded")
        constants_ready = sem("constants_ready")
        buffers_clean = sem("buffers_clean")
        own_ready = sem("own_ready")
        counts_ready = sem("counts_ready")
        ranks_ready = sem("ranks_ready")
        slots_ready = sem("slots_ready")
        slots_summed = sem("slots_summed")
        rows_ready = sem("rows_ready")
        tables_ready = sem("tables_ready")
        route_step = sem("route_step")
        row_copied = sem("row_copied")
        x_loaded = [sem(f"x_loaded{s}") for s in range(UNROLL)]
        stored = [sem(f"stored{s}") for s in range(UNROLL)]
        w_loaded = [sem(f"w_loaded{h}") for h in range(HALVES)]
        xt_ready = sem("xt_ready")
        hi_ready = sem("hi_ready")
        lo_ready = sem("lo_ready")
        product_ready = sem("product_ready")
        out_added = sem("out_added")
        w_turned = sem("w_turned")
        w_hi_ready = sem("w_hi_ready")
        w_lo_ready = sem("w_lo_ready")

        def done(n):
            return n + CREDIT

        def load_half(eng, a, h):
            for k in range(KG):
                eng.dma_start(w_raw[h][Q * k:Q * k + Q, :, :],
                              weight_v[bass.ds(a, 1), h, k, :, :, :].rearrange("a o m i -> (a o) m i")
                              ).then_inc(w_loaded[h], 16)

        CONSTANTS = {"ones": 1, "adapter_no": 2, "earlier": 3, "slot_no": 4, "seq_off": 5, "row_in_seq": 6, "identity": 7}

        def quarter(w, j, n):
            h, u = n // 2, n % 2
            at = w[:, bass.ds(j, 1), 2 * u:2 * u + 2, h * HO:(h + 1) * HO]
            return at.rearrange("p a c o -> p (a c) o")

        block = ctx.enter_context(nc.Block())

        @block.sync
        def _(sp):
            for s in (xt_ready, hi_ready, lo_ready, product_ready, out_added, w_turned, w_hi_ready, w_lo_ready):
                sp.sem_inc(s, CREDIT)
            sp.dma_start(ids_i[:, :], ids.rearrange("(b o) -> b o", o=1)).then_inc(ids_loaded, 16)
            sp.wait_ge(ranks_ready, 1)
            first = sp.value_load(adapter_of_rank[0:1, 0:1], min_val=0, max_val=ADAPTERS - 1)
            load_half(sp, first, 0)
            with sp.Fori(1, ADAPTERS) as j:
                a = sp.value_load(adapter_of_rank[0:1, bass.ds(j, 1)], min_val=0, max_val=ADAPTERS - 1)
                for h in range(HALVES):
                    sp.wait_ge(w_turned, done(j * QUARTERS - QUARTERS + 2 * h + 2))
                    load_half(sp, a, h)

        @block.gpsimd
        def _(pool):
            def iota(out_, pattern, base, per_partition):
                nc.gpsimd.iota(out_, pattern, base=base, channel_multiplier=per_partition,
                               allow_small_or_imprecise_dtypes=True).then_inc(constants_ready, 1)

            nc.gpsimd.memset(ones[:, :], 1.0).then_inc(constants_ready, 1)
            iota(adapter_no[:, :], [[1, ADAPTERS]], 0, 0)
            pool.wait_ge(constants_ready, CONSTANTS["ones"])
            nc.gpsimd.affine_select(out=earlier[:, :], in_=ones[:, :], compare_op=ALU.is_ge, fill=0.0,
                                    base=-1, pattern=[[1, P]], channel_multiplier=-1).then_inc(constants_ready, 1)
            iota(slot_no[:, :], [[1, SEQS * TABLE]], 0, 0)
            iota(seq_off[:, :], [[0, P]], -B, 1)
            nc.gpsimd.iota(row_in_seq[:, :], [[0, 1]], base=0, channel_multiplier=1).then_inc(constants_ready, 1)
            nc.gpsimd.memset(identity[:, :], 0.0).then_inc(row_copied, 1)
            pool.wait_ge(row_copied, 1)
            nc.gpsimd.affine_select(out=identity[:, :], in_=identity[:, :], compare_op=ALU.not_equal, fill=1.0,
                                    base=0, pattern=[[-1, P]], channel_multiplier=1).then_inc(constants_ready, 1)

            def gather(s, rows):
                nc.gpsimd.indirect_dma_start(
                    out=x_tile[s][:, :], out_offset=None, in_=x_rows,
                    in_offset=bass.IndirectOffsetOnAxis(ap=rows, axis=0),
                    bounds_check=NO_ROW - 1, oob_is_err=False).then_inc(x_loaded[s], 16)

            def scatter(s, rows):
                nc.gpsimd.indirect_dma_start(
                    out=out_rows, out_offset=bass.IndirectOffsetOnAxis(ap=rows, axis=0),
                    in_=out_tile[s][:, :], in_offset=None,
                    bounds_check=NO_ROW - 1, oob_is_err=False).then_inc(stored[s], 16)

            def take_rows(t, s, round_no):
                pool.wait_ge(stored[s], 16 * round_no)
                nc.gpsimd.tensor_copy(row_now[s][:, :], row_of[:, bass.ds(t, 2, AHEAD)]).then_inc(row_copied, 1)

            pool.wait_ge(rows_ready, 1)
            pool.wait_ge(buffers_clean, UNROLL)
            for s in range(UNROLL):
                gather(s, row_of[:, s:s + 1])
            take_rows(0, 0, 0)

            def start_step(t, s, round_no):
                pool.wait_ge(out_added, done(t + 1))
                pool.wait_ge(row_copied, t + 2)
                if not (isinstance(t, int) and t + 1 == MAX_TILES):
                    take_rows(t + 1, (s + 1) % UNROLL, round_no + (s + 1) // UNROLL)

            with pool.Fori(0, W_ROUNDS) as r:
                for s in range(UNROLL):
                    start_step(r * UNROLL + s, s, r)
                    gather(s, row_now[s][:, 1:2])
                    scatter(s, row_now[s][:, 0:1])
            tiles = pool.value_load(tile_count[0:1, 0:1], min_val=MIN_TILES, max_val=MAX_TILES)

            def last_step(t):
                s = t % UNROLL
                start_step(t, s, t // UNROLL)
                if t + AHEAD < MAX_TILES:
                    with pool.If(tiles > t + AHEAD):
                        gather(s, row_now[s][:, 1:2])
                scatter(s, row_now[s][:, 0:1])

            for t in range(W_ROUNDS * UNROLL, MIN_TILES):
                last_step(t)
            for t in range(MIN_TILES, MAX_TILES):
                with pool.If(tiles > t):
                    last_step(t)
            for s in range(UNROLL):
                pool.wait_ge(stored[s], 16 * ((tiles + (UNROLL - 1 - s)) >> 2))

        @block.scalar
        def _(act):
            act.wait_ge(constants_ready, CONSTANTS["ones"])
            nc.scalar.activation(warm[:, :], ones[0:1, 0:1], COPY)
            act.wait_ge(ranks_ready, 1)
            load_half(act, act.value_load(adapter_of_rank[0:1, 0:1], min_val=0, max_val=ADAPTERS - 1), 1)

            def split_x(t, s):
                act.wait_ge(xt_ready, done(t + 1))
                act.wait_ge(product_ready, done(t - 1))
                nc.scalar.activation(xt_hi[s % 2][:, :, :], xt_ps[s % 2][:, :, :], COPY).then_inc(hi_ready, 1)

            def split_weight(j, n):
                act.wait_ge(w_turned, done(j * QUARTERS + n + 1))
                nc.scalar.activation(quarter(w_hi, j, n), w_ps[n % 2][:, :, :], COPY).then_inc(w_hi_ready, 1)

            for n in range(QUARTERS):
                split_weight(0, n)
            split_x(0, 0)
            with act.Fori(0, W_ROUNDS) as r:
                for s in range(UNROLL):
                    split_x(r * UNROLL + s + 1, s + 1)
                    split_weight(r + 1, s)
            for t in range(W_ROUNDS * UNROLL + 1, MIN_TILES):
                split_x(t, t)
            tiles = act.value_load(tile_count[0:1, 0:1], min_val=MIN_TILES, max_val=MAX_TILES)
            for t in range(MIN_TILES, MAX_TILES):
                with act.If(tiles > t):
                    split_x(t, t)

        @block.vector
        def _(dve):
            steps = [0]

            def link(ins):
                steps[0] += 1
                ins.then_inc(route_step, 1)
                dve.wait_ge(route_step, steps[0])

            for s in range(UNROLL):
                nc.vector.memset(x_tile[s][:, :], 0.0).then_inc(buffers_clean, 1)
            dve.wait_ge(ids_loaded, 16)
            dve.wait_ge(constants_ready, CONSTANTS["adapter_no"])
            nc.vector.tensor_scalar(is_own[:, :], adapter_no[:, :], ids_i[:, 0:1], None, ALU.is_equal).then_inc(own_ready, 1)
            dve.wait_ge(constants_ready, CONSTANTS["row_in_seq"])
            link(nc.vector.tensor_scalar(row_in_seq[:, :], row_in_seq[:, :], S - 1, None, ALU.bitwise_and))
            link(nc.vector.tensor_scalar(row_base[:, :], row_in_seq[:, :], float(NO_ROW), None, ALU.add))
            dve.wait_ge(counts_ready, 1)
            link(nc.vector.tensor_scalar(tiles_i[:, :], counts, 1.0 / SEQS, 0.375, ALU.mult, ALU.add))
            link(nc.vector.scalar_tensor_tensor(out=key[:, :], in0=tiles_i[:, :], scalar=float(KEY),
                                                in1=adapter_no[:, :], op0=ALU.mult, op1=ALU.add))
            link(nc.vector.max(sorted_key[0:1, :], key[0:1, :]))
            nc.vector.tensor_scalar(adapter_of_rank[0:1, :], sorted_key[0:1, :], KEY - 1, None,
                                    ALU.bitwise_and).then_inc(ranks_ready, 1)
            link(nc.vector.tensor_tensor_reduce(out=masked[:, :], in0=key[:, :], in1=is_own[:, :], scale=1.0,
                                                scalar=0.0, op0=ALU.mult, op1=ALU.add, accum_out=own_key[:, 0:1]))
            link(nc.vector.tensor_scalar(masked[:, :], key[:, :], own_key[:, 0:1], None, ALU.is_gt))
            link(nc.vector.tensor_tensor_reduce(out=key[:, :], in0=masked[:, :], in1=tiles_i[:, :], scale=float(SEQS),
                                                scalar=0.0, op0=ALU.mult, op1=ALU.add, accum_out=start_slot[:, 0:1]))
            link(nc.vector.tensor_tensor_reduce(out=key[:, :], in0=earlier_own, in1=is_own[:, :], scale=1.0,
                                                scalar=start_slot[:, 0:1], op0=ALU.mult, op1=ALU.add,
                                                accum_out=slot[:, 0:1]))
            nc.vector.tensor_scalar(in_slot[:, :], slot_no[:, :], slot[:, 0:1], None, ALU.is_equal).then_inc(slots_ready, 1)
            link(nc.vector.tensor_reduce(out=own_rank[:, :], in_=masked[:, :], axis=mybir.AxisListType.X, op=ALU.add))
            nc.vector.tensor_copy(own_rank_b[:, :], own_rank[:, :]).then_inc(slots_ready, 1)
            link(nc.vector.tensor_reduce(out=tiles_f[0:1, :], in_=tiles_i[0:1, :], axis=mybir.AxisListType.X, op=ALU.add))
            nc.vector.tensor_copy(tile_count[0:1, :], tiles_f[0:1, :]).then_inc(tables_ready, 1)
            dve.wait_ge(slots_summed, 1)
            by_place = seq_of_slot.rearrange("p (t m) -> p m t", m=SEQS)
            for m in range(SEQS):
                rows = slice(S * m, S * m + S)
                last = nc.vector.tensor_scalar(row_of[rows, :], by_place[rows, m, :], float(S), row_base[rows, 0:1],
                                               ALU.mult, ALU.add)
            last.then_inc(rows_ready, 1)
            dve.wait_ge(slots_summed, 2)
            nc.vector.tensor_copy(rank_of_tile[0:1, :], rank_sums).then_inc(tables_ready, 1)

            def split_x(t, s):
                dve.wait_ge(hi_ready, done(t + 1))
                nc.vector.tensor_tensor(xt_lo[s % 2][:, :, :], xt_ps[s % 2][:, :, :],
                                        xt_hi[s % 2][:, :, :].bitcast(f32), ALU.subtract).then_inc(lo_ready, 1)

            def turn_weight(j, n):
                h, u = n // 2, n % 2
                dve.wait_ge(w_loaded[h], j * (16 * KG) + 16 * KG)
                dve.wait_ge(w_lo_ready, done(j * QUARTERS + n - 1))
                nc.vector.transpose(
                    w_ps[n % 2][:, :, :].rearrange("p c (m o) -> p c m o", o=Q),
                    w_raw[h][:, :, :].rearrange("p m (q c) -> p c m q", c=CHUNKS)[:, 2 * u:2 * u + 2, :, :]
                ).then_inc(w_turned, 1)

            def split_weight(j, n):
                dve.wait_ge(w_hi_ready, done(j * QUARTERS + n + 1))
                nc.vector.tensor_tensor(quarter(w_lo, j, n), w_ps[n % 2][:, :, :], quarter(w_hi, j, n).bitcast(f32),
                                        ALU.subtract).then_inc(w_lo_ready, 1)

            def add_x(t, s, round_no):
                dve.wait_ge(product_ready, done(t + 1))
                dve.wait_ge(stored[s], round_no * 16)
                nc.vector.tensor_tensor(out_tile[s][:, :], out_ps[s][:, :], x_tile[s][:, :],
                                        ALU.add).then_inc(out_added, 1)

            turn_weight(0, 0)
            for n in range(QUARTERS):
                if n + 1 < QUARTERS:
                    turn_weight(0, n + 1)
                split_weight(0, n)
            split_x(0, 0)
            with dve.Fori(0, W_ROUNDS) as r:
                for s in range(UNROLL):
                    turn_weight(r + 1, s)
                    split_x(r * UNROLL + s + 1, s + 1)
                    split_weight(r + 1, s)
                    add_x(r * UNROLL + s, s, r)
            tiles = dve.value_load(tile_count[0:1, 0:1], min_val=MIN_TILES, max_val=MAX_TILES)

            def last_step(t):
                if t + 1 < MIN_TILES:
                    split_x(t + 1, t + 1)
                elif t + 1 < MAX_TILES:
                    with dve.If(tiles > t + 1):
                        split_x(t + 1, t + 1)
                add_x(t, t % UNROLL, t // UNROLL)

            for t in range(W_ROUNDS * UNROLL, MIN_TILES):
                last_step(t)
            for t in range(MIN_TILES, MAX_TILES):
                with dve.If(tiles > t):
                    last_step(t)

        @block.tensor
        def _(pe):
            pe.wait_ge(constants_ready, CONSTANTS["earlier"])
            pe.wait_ge(own_ready, 1)
            nc.tensor.matmul(counts, ones[:, :], is_own[:, :], start=True, stop=True)
            nc.tensor.matmul(earlier_own, earlier[:, :], is_own[:, :], start=True, stop=True).then_inc(counts_ready, 1)
            pe.wait_ge(constants_ready, CONSTANTS["seq_off"])
            pe.wait_ge(slots_ready, 1)
            nc.tensor.matmul(seq_of_slot, seq_off[:, :], in_slot[:, :], start=True, stop=True).then_inc(slots_summed, 1)
            pe.wait_ge(slots_ready, 2)
            nc.tensor.matmul(rank_sums, own_rank_b[:, :], in_slot[:, :].rearrange("b (t m) -> b m t", m=SEQS)[:, 0, :],
                             start=True, stop=True).then_inc(slots_summed, 1)

            def transpose_x(t, s, round_no):
                pe.wait_ge(x_loaded[s], round_no * 16 + 16)
                pe.wait_ge(lo_ready, done(t - 1))
                rows = x_tile[s][:, :].rearrange("r (j c) -> r c j", c=CHUNKS)
                for c in range(CHUNKS):
                    last = nc.tensor.transpose(xt_ps[s % 2][:, c, :], rows[:, c, :], identity[:, :])
                last.then_inc(xt_ready, 1)

            def multiply(t, s, rank):
                pe.wait_ge(w_lo_ready, done(rank * QUARTERS + QUARTERS))
                pe.wait_ge(lo_ready, done(t + 1))
                pe.wait_ge(out_added, done(t - 3))
                for c in range(CHUNKS):
                    for n, (left, right) in enumerate(((xt_hi, w_hi), (xt_lo, w_hi), (xt_hi, w_lo))):
                        last = nc.tensor.matmul(out_ps[s][:, :], left[s % 2][:, c, :],
                                                right[:, bass.ds(rank, 1), c, :].rearrange("p a o -> p (a o)"),
                                                start=(c == 0 and n == 0), stop=(c == CHUNKS - 1 and n == 2))
                last.then_inc(product_ready, 1)

            def rank_of(t):
                return pe.value_load(rank_of_tile[0:1, bass.ds(t, 1)], min_val=0, max_val=ADAPTERS - 1)

            pe.wait_ge(constants_ready, CONSTANTS["identity"])
            pe.wait_ge(tables_ready, 2)
            transpose_x(0, 0, 0)
            with pe.Fori(0, W_ROUNDS) as r:
                for s in range(UNROLL):
                    t = r * UNROLL + s
                    rank = rank_of(t)
                    transpose_x(t + 1, (s + 1) % UNROLL, r + (s + 1) // UNROLL)
                    multiply(t, s, rank)
            tiles = pe.value_load(tile_count[0:1, 0:1], min_val=MIN_TILES, max_val=MAX_TILES)

            def last_step(t):
                rank = rank_of(t)
                if t + 1 < MIN_TILES:
                    transpose_x(t + 1, (t + 1) % UNROLL, (t + 1) // UNROLL)
                elif t + 1 < MAX_TILES:
                    with pe.If(tiles > t + 1):
                        transpose_x(t + 1, (t + 1) % UNROLL, (t + 1) // UNROLL)
                multiply(t, t % UNROLL, rank)

            for t in range(W_ROUNDS * UNROLL, MIN_TILES):
                last_step(t)
            for t in range(MIN_TILES, MAX_TILES):
                with pe.If(tiles > t):
                    last_step(t)


def kernel(**inputs):
    import concourse.bacc as bacc
    from concourse.bass_utils import run_bass_kernel_spmd

    nc = bacc.Bacc("TRN2", target_bir_lowering=False, num_devices=1)
    arrays, args = {}, []
    for name in ("x", "itok_B_3_7", "L0_cond_weight"):
        a = np.ascontiguousarray(inputs[name])
        arrays[f"in_{name}"] = a
        args.append(nc.dram_tensor(f"in_{name}", a.shape, mybir.dt.from_np(a.dtype), kind="ExternalInput").ap())
    out = nc.dram_tensor("out", (B, S, D), mybir.dt.float32, kind="ExternalOutput").ap()
    routed_adapter_kernel(nc, *args, out)
    result = run_bass_kernel_spmd(nc, [arrays], core_ids=[0])
    return result.results[0]["out"]
```
